# Optimizing a Trainium2 kernel written in Bass

```python
import numpy as np
import jax
import jax.numpy as jnp

def _softmax(x, axis=-1):
    return jax.nn.softmax(x, axis=axis)

def _gelu(x):
    return jax.nn.gelu(x, approximate=True)

def _silu(x):
    return jax.nn.silu(x)

def _sigmoid(x):
    return jax.nn.sigmoid(x)

def _layernorm(x, axis=-1, eps=1e-05):
    m = jnp.mean(x, axis=axis, keepdims=True)
    v = jnp.var(x, axis=axis, keepdims=True)
    return (x - m) / jnp.sqrt(v + eps)

def _scatter_add(tgt, idx, src, axis=0):
    return tgt.at[idx].add(src)

def _segment_sum(src, seg, n):
    return jax.ops.segment_sum(src, seg, n)
kernel_name = 'mk_adj_resnorm_d1_adj_r2_08d6ef'

def setup_inputs(seed: int=0):
    np.random.seed(seed)
    _w = jnp.asarray

    def _rec_inputs():
        import jax
        import jax.numpy as jnp
        _gk = jax.random.key(seed)
        x = -0.0004039 + 1 * jax.random.normal(jax.random.fold_in(_gk, 1), (64, 128, 384), jnp.float32)
        _a = jax.random.bernoulli(jax.random.fold_in(_gk, 2), 0.03125, (64, 128, 128))
        _a = jnp.logical_or(_a, jnp.swapaxes(_a, -1, -2))
        _a = jnp.logical_or(_a, jnp.eye(128, dtype=bool))
        _af = _a.astype(jnp.float32)
        adj = _af
        return (x, adj)
    x, adj = _rec_inputs()

    def _L0_gnn_setup():
        import jax, jax.numpy as jnp
        import numpy as np
        B, S, H, L = (32, 256, 384, 2)

        def _layer_norm(z, a, b, eps=0.001):
            mu = jnp.mean(z, axis=-1, keepdims=True)
            sigma = jnp.std(z, axis=-1, keepdims=True, ddof=1)
            return (z - mu) / (sigma + eps) * a + b
        key = jax.random.key(seed)
        ks = jax.random.split(key, 6)
        hidden_state = jax.random.normal(ks[0], (B, S, H), dtype=jnp.float32)
        adjacency_matrix = (jax.random.uniform(ks[1], (B, S, S)) < 0.2).astype(jnp.float32)
        W_left = 0.05 * jax.random.normal(ks[2], (L, H, H), dtype=jnp.float32)
        W_right = 0.05 * jax.random.normal(ks[3], (L, H, H), dtype=jnp.float32)
        W_lin = 0.05 * jax.random.normal(ks[4], (L, H, H), dtype=jnp.float32)
        b_lin = jnp.zeros((L, H), dtype=jnp.float32)
        ln_a = jnp.ones((L, H), dtype=jnp.float32)
        ln_b = jnp.zeros((L, H), dtype=jnp.float32)
        return {'hidden_state': hidden_state, 'adjacency_matrix': adjacency_matrix, 'W_left': W_left, 'W_right': W_right, 'W_lin': W_lin, 'b_lin': b_lin, 'ln_a': ln_a, 'ln_b': ln_b}
    _L0_gnn_all = _L0_gnn_setup()
    _L0_gnn_in = {k: v for k, v in _L0_gnn_all.items() if k in ('W_left', 'W_right', 'W_lin', 'b_lin', 'ln_a', 'ln_b')}
    del _L0_gnn_all
    return {'x': x, 'adj': adj, 'L0_gnn_W_left': _L0_gnn_in['W_left'], 'L0_gnn_W_right': _L0_gnn_in['W_right'], 'L0_gnn_W_lin': _L0_gnn_in['W_lin'], 'L0_gnn_b_lin': _L0_gnn_in['b_lin'], 'L0_gnn_ln_a': _L0_gnn_in['ln_a'], 'L0_gnn_ln_b': _L0_gnn_in['ln_b']}

def reference(x, adj, L0_gnn_W_left, L0_gnn_W_right, L0_gnn_W_lin, L0_gnn_b_lin, L0_gnn_ln_a, L0_gnn_ln_b):
    import jax
    import jax.numpy as jnp

    def _L0_gnn_ref(hidden_state, adjacency_matrix, W_left, W_right, W_lin, b_lin, ln_a, ln_b):
        import jax, jax.numpy as jnp
        import numpy as np
        B, S, H, L = (32, 256, 384, 2)

        def _layer_norm(z, a, b, eps=0.001):
            mu = jnp.mean(z, axis=-1, keepdims=True)
            sigma = jnp.std(z, axis=-1, keepdims=True, ddof=1)
            return (z - mu) / (sigma + eps) * a + b
        temper = float(np.sqrt(H))
        adj = adjacency_matrix
        adj_tri = jnp.triu(adj, k=1)
        diag_mask = jnp.triu(adj, k=0) - adj_tri
        h = hidden_state
        for l in range(L):
            m_left = jnp.einsum('bsh,oh->bso', h, W_left[l])
            m_right = jnp.einsum('bsh,oh->bso', h, W_right[l])
            u_left = jnp.einsum('bih,bjh->bij', h, m_left) / temper
            u_right = jnp.einsum('bih,bjh->bij', h, m_right) / temper
            u = u_left * adj_tri + u_left * diag_mask + u_right * jnp.swapaxes(adj_tri, 1, 2)
            delta_exp_u = jnp.exp(u) * adj
            attention = delta_exp_u / (jnp.sum(delta_exp_u, axis=2, keepdims=True) + 1e-10)
            h_lin = jnp.einsum('bsh,oh->bso', h, W_lin[l]) + b_lin[l]
            ctx = jnp.matmul(attention, h_lin)
            h = jax.nn.relu(_layer_norm(ctx, ln_a[l], ln_b[l]))
        return h
    x = _layernorm(x + _L0_gnn_ref(x, adj, L0_gnn_W_left, L0_gnn_W_right, L0_gnn_W_lin, L0_gnn_b_lin, L0_gnn_ln_a, L0_gnn_ln_b), axis=-1)
    return x

_drawn_inputs = setup_inputs


def setup_inputs(seed=0):
    import zlib

    import numpy as np

    out = dict(_drawn_inputs(seed))
    spreads = {'L0_gnn_b_lin': (0.0, 0.1), 'L0_gnn_ln_a': (1.0, 0.2), 'L0_gnn_ln_b': (0.0, 0.1)}
    factors = {}
    for name, (base, spread) in spreads.items():
        noise = np.random.default_rng([zlib.crc32(name.encode()), seed]).standard_normal(out[name].shape)
        drawn = base * np.exp(spread * noise) if base else spread * noise
        out[name] = jnp.asarray(drawn.astype(out[name].dtype))
    for name, factor in factors.items():
        out[name] = (out[name] * factor).astype(out[name].dtype)
    return out
```

```python
from contextlib import ExitStack

import numpy as np

import concourse.bass as bass
from concourse import mybir

F32 = mybir.dt.float32
F32R = mybir.dt.float32r
ALU = mybir.AluOpType
ACT = mybir.ActivationFunctionType

P = 128
H = 384
KT = H // P
LAYERS = 2
NG = 4
NODES = NG * P
SIDES = 2
QT = SIDES * KT
PAIRS = NG // 2
VW = H + 2
BANK = 512
DMA = 16
LN_EPS = 1e-3
SUM_EPS = 1e-10
OUT_EPS = 1e-5
UNBIASED = float(np.sqrt(H / (H - 1.0)))
SCORE_SCALE = 1.0 / float(np.sqrt(H))


def build_gnn(nc, x_t, x_rows, edges_dram, weights, ln_cols, ln_rows, bias_rows, out):
    groups = x_t.shape[0]
    last = groups - 1

    with ExitStack() as ctx:
        def sb(name, shape, dt=F32):
            return ctx.enter_context(nc.sbuf_tensor(name, shape, dt))

        def sem(name):
            return ctx.enter_context(nc.semaphore(name))

        w_hi = sb("w_hi", [P, LAYERS, 3, KT, H], F32R)
        w_lo = sb("w_lo", [P, LAYERS, 3, KT, H], F32R)
        x_raw = sb("x_raw", [P, KT, NODES])
        feat_hi = [sb(f"feat_hi{l}", [P, KT, NODES], F32R) for l in range(LAYERS)]
        feat_lo = [sb(f"feat_lo{l}", [P, KT, NODES], F32R) for l in range(LAYERS)]
        h_full = sb("h_full", [P, KT, NODES])
        q_hi = sb("q_hi", [P, KT, NG, SIDES, P], F32R)
        q_lo = sb("q_lo", [P, KT, NG, SIDES, P], F32R)
        v_full = sb("v_full", [P, NG, H])
        v_hi = sb("v_hi", [P, NG, VW], F32R)
        v_lo = sb("v_lo", [P, NG, VW], F32R)
        edges = [sb(f"edges{b}", [P, NG, 2, P]) for b in range(2)]
        masks = [sb(f"masks{b}", [P, NG, SIDES, P]) for b in range(2)]
        u_masked = sb("u_masked", [P, NG, SIDES, P])
        attn = sb("attn", [P, NG, P])
        p_hi = sb("p_hi", [P, NG, P], F32R)
        p_lo = sb("p_lo", [P, NG, P], F32R)
        c_rows = sb("c_rows", [P, NG, VW])
        xhat = sb("xhat", [P, NG, H])
        z = sb("z", [P, NG, H])
        x_res = sb("x_res", [P, NG, H])
        o_rows = sb("o_rows", [P, NG, H])
        identity = sb("identity", [P, P])
        ones = sb("ones", [P, P])
        triangles = sb("triangles", [P, SIDES, P])
        half = sb("half", [P, NG])
        minus_half = sb("minus_half", [P, NG])
        ln_col = sb("ln_col", [P, 2, KT])
        ln_row = sb("ln_row", [P, 2, H])
        bias_row = sb("bias_row", [P, LAYERS, H])
        stats = sb("stats", [P, NG, 6])
        mean_var = sb("mean_var", [P, NG, 2])
        sum_eps = sb("sum_eps", [P, NG])
        sd = sb("sd", [P, NG])
        den = sb("den", [P, NG])
        scale = sb("scale", [P, NG])
        z_stats = sb("z_stats", [P, NG, 6])
        z_mean_var = sb("z_mean_var", [P, NG, 2])
        z_var = sb("z_var", [P, NG])
        z_rstd = sb("z_rstd", [P, NG])

        def staging(buffer):
            return buffer.rearrange("p a b -> p (a b)")[:, 0:KT * H]

        w_stage = [staging(b) for b in (xhat[:], z[:], o_rows[:], x_res[:], c_rows[:], h_full[:])]
        MATS = len(w_stage)

        q_ps = ctx.enter_context(nc.psum_tensor("q_ps", [P, 2, BANK], F32))
        vu_ps = ctx.enter_context(nc.psum_tensor("vu_ps", [P, 3, BANK], F32))
        c_ps = ctx.enter_context(nc.psum_tensor("c_ps", [P, 3, BANK], F32))

        w_loaded = [sem(f"w_loaded{i}") for i in range(MATS)]
        x_loaded = sem("x_loaded")
        const_loaded = sem("const_loaded")
        edges_loaded = [sem(f"edges_loaded{b}") for b in range(2)]
        res_loaded = sem("res_loaded")
        stored = sem("stored")
        q_done = sem("q_done")
        v_done = sem("v_done")
        u_done = sem("u_done")
        c_done = sem("c_done")
        turned = sem("turned")
        w_hi_done = sem("w_hi_done")
        w_lo_done = sem("w_lo_done")
        x_hi_done = sem("x_hi_done")
        feat_ready = [sem(f"feat_ready{l}") for l in range(LAYERS)]
        h_full_done = sem("h_full_done")
        h_hi_done = sem("h_hi_done")
        q_hi_done = sem("q_hi_done")
        q_lo_done = sem("q_lo_done")
        v_sum_done = sem("v_sum_done")
        v_hi_done = sem("v_hi_done")
        v_lo_done = sem("v_lo_done")
        masked_done = sem("masked_done")
        u_sum_done = sem("u_sum_done")
        exp_done = sem("exp_done")
        p_done = sem("p_done")
        p_hi_done = sem("p_hi_done")
        p_lo_done = sem("p_lo_done")
        masks_ready = sem("masks_ready")
        c_copied = sem("c_copied")
        c_stats_done = sem("c_stats_done")
        c_aggr_done = sem("c_aggr_done")
        sd_done = sem("sd_done")
        den_done = sem("den_done")
        norm_done = sem("norm_done")
        z_scaled = sem("z_scaled")
        z_affine_done = sem("z_affine_done")
        z_res_done = sem("z_res_done")
        z_stats_done = sem("z_stats_done")
        z_aggr_done = sem("z_aggr_done")
        z_rstd_done = sem("z_rstd_done")
        o_done = sem("o_done")
        consts_set = sem("consts_set")
        blank_done = sem("blank_done")

        CONSTS = 8

        def wait(eng, semaphore, value):
            if not isinstance(value, int) or value > 0:
                eng.wait_ge(semaphore, value)

        def nodes(g):
            return slice(g * P, (g + 1) * P)

        def each_turn(eng, first, steady):
            first(0)
            first(1)
            with eng.Fori(1, groups // 2 - 1) as pair:
                for b in range(2):
                    steady(2 * pair + b, b, pair)
            for t in (last - 1, last):
                steady(t, t % 2, t // 2)

        block = ctx.enter_context(nc.Block())

        @block.sync
        def _(sp):
            def load_edges(t, b):
                if not isinstance(t, int) or t >= 2:
                    wait(sp, p_done, PAIRS * (2 * t - 1))
                sp.dma_start(edges[b][:], edges_dram[t]).then_inc(edges_loaded[b], DMA)

            def load_x(g):
                wait(sp, feat_ready[0], KT * g)
                sp.dma_start(x_raw[:], x_t[g]).then_inc(x_loaded, DMA)

            def load_res(g):
                wait(sp, z_res_done, NG * g)
                sp.dma_start(x_res[:], x_rows[g]).then_inc(res_loaded, DMA)

            def store(g):
                wait(sp, o_done, NG * (g + 1))
                sp.dma_start(out[g], o_rows[:]).then_inc(stored, DMA)

            def load_weights(i):
                sp.dma_start(w_stage[i], weights[i]).then_inc(w_loaded[i], DMA)

            load_x(0)
            load_weights(0)
            load_weights(1)
            load_weights(2)
            sp.dma_start(bias_row[:], bias_rows).then_inc(const_loaded, DMA)
            load_edges(0, 0)
            load_edges(1, 1)
            sp.dma_start(ln_col[:], ln_cols).then_inc(const_loaded, DMA)
            sp.dma_start(ln_row[:], ln_rows).then_inc(const_loaded, DMA)
            for i in range(3, MATS):
                load_weights(i)

            def first(t):
                load_x(t + 1)
                if t == 1:
                    sp.wait_ge(w_lo_done, MATS)

            def steady(t, b, half_t):
                load_edges(t, b)
                load_res(t - 2)
                if not (isinstance(t, int) and t == last):
                    load_x(t + 1)
                store(t - 2)

            each_turn(sp, first, steady)
            load_res(last - 1)
            load_res(last)
            store(last - 1)
            store(last)
            sp.wait_ge(stored, DMA * groups)

        @block.tensor
        def _(pe):
            def product(out_ap, left, right, start, stop):
                (l_hi, l_lo), (r_hi, r_lo) = left, right
                pe.matmul(out_ap, l_hi, r_hi, start=start, stop=False)
                pe.matmul(out_ap, l_hi, r_lo, start=False, stop=False)
                return pe.matmul(out_ap, l_lo, r_hi, start=False, stop=stop)

            def queries(n, l, grp, m):
                wait(pe, q_lo_done, QT * n + m - 1)
                side, mt = divmod(m, KT)
                for k in range(KT):
                    if m == 0:
                        wait(pe, feat_ready[l], KT * grp + k + 1)
                    if isinstance(n, int) and n in (0, 2) and mt == 0 and k == 0:
                        pe.wait_ge(w_lo_done, 3 * l + side + 1)
                    cols = slice(mt * P, (mt + 1) * P)
                    mm = product(q_ps[:, m % 2, :],
                                 (w_hi[:, l, side, k, cols], w_lo[:, l, side, k, cols]),
                                 (feat_hi[l][:, k, :], feat_lo[l][:, k, :]), k == 0, k == KT - 1)
                mm.then_inc(q_done, 1)

            def values(n, l, g):
                if g == 0:
                    wait(pe, v_sum_done, NG * n)
                elif g == 3:
                    pe.wait_ge(v_sum_done, NG * n + 1)
                else:
                    wait(pe, masked_done, PAIRS * n + g - 2)
                if isinstance(n, int) and n in (0, 2) and g == 0:
                    pe.wait_ge(w_lo_done, 3 * l + 3)
                for k in range(KT):
                    mm = product(vu_ps[:, g % 3, 0:H],
                                 (feat_hi[l][:, k, nodes(g)], feat_lo[l][:, k, nodes(g)]),
                                 (w_hi[:, l, 2, k, :], w_lo[:, l, 2, k, :]), k == 0, k == KT - 1)
                mm.then_inc(v_done, 1)

            def scores(n, l, pair):
                if pair == 0:
                    pe.wait_ge(q_lo_done, QT * (n + 1))
                pe.wait_ge(v_sum_done, NG * n + 2 + pair)
                for g in (2 * pair, 2 * pair + 1):
                    at = (g % 2) * SIDES * P
                    for k in range(KT):
                        mm = product(vu_ps[:, 1 + pair, at:at + SIDES * P],
                                     (feat_hi[l][:, k, nodes(g)], feat_lo[l][:, k, nodes(g)]),
                                     (q_hi[:, k, g], q_lo[:, k, g]), k == 0, k == KT - 1)
                mm.then_inc(u_done, 1)

            def context(c, g, turned_groups):
                if g == 0:
                    wait(pe, c_copied, NG * c)
                    wait(pe, h_full_done, KT * turned_groups)
                if g == 3:
                    pe.wait_ge(c_copied, NG * c + 1)
                if g % 2 == 0:
                    pe.wait_ge(p_lo_done, PAIRS * c + g // 2 + 1)
                pe.wait_ge(v_lo_done, NG * c + g + 1)
                product(c_ps[:, g % 3, 0:VW], (p_hi[:, g, :], p_lo[:, g, :]),
                        (v_hi[:, g, :], v_lo[:, g, :]), True, True).then_inc(c_done, 1)

            def turn(grp, contexts):
                pe.wait_ge(c_copied, NG * contexts)
                pe.wait_ge(norm_done, NG * contexts)
                for k in range(KT):
                    for g in range(NG):
                        tr = pe.transpose(c_ps[:, k, nodes(g)], xhat[:, g, k * P:(k + 1) * P], identity[:])
                    tr.then_inc(turned, 1)

            def phase(n, l, grp, prev, turned_groups, turn_at=None):
                for m in range(QT):
                    if turn_at and turn_at[0] == m:
                        turn(*turn_at[1:])
                    queries(n, l, grp, m)
                for g in range(NG):
                    if prev:
                        context(n - 1, g, turned_groups)
                    values(n, l, g)
                for pair in range(PAIRS):
                    scores(n, l, pair)

            def first(t):
                if t == 0:
                    pe.wait_ge(consts_set, CONSTS)
                    phase(0, 0, 0, False, 0)
                else:
                    phase(1, 0, 1, True, 0)
                    phase(2, 1, 0, True, 1, (0, 0, 1))

            def steady(t, b, half_t):
                n = 2 * t - 1
                phase(n, 0, t, True, t, (3, t - 1, n - 1))
                phase(n + 1, 1, t - 1, True, t)

            each_turn(pe, first, steady)
            end = 2 * last + 1
            phase(end, 1, last, True, groups, (0, last, end - 1))
            for g in range(NG):
                context(end, g, groups)

        @block.scalar
        def _(act):
            def split_weights(i):
                act.wait_ge(w_loaded[i], DMA)
                act.activation(w_hi[:, i // 3, i % 3].rearrange("p a b -> p (a b)"), w_stage[i],
                               ACT.Copy).then_inc(w_hi_done, 1)

            def split_x(grp, k, scores_before):
                if k == 0:
                    wait(act, x_loaded, DMA * (grp + 1))
                    wait(act, u_done, scores_before)
                act.activation(feat_hi[0][:, k, :], x_raw[:, k, :], ACT.Copy).then_inc(x_hi_done, 1)

            def split_queries(n, m):
                side, mt = divmod(m, KT)
                if m == 0:
                    wait(act, u_done, PAIRS * n)
                act.wait_ge(q_done, QT * n + m + 1)
                act.activation(q_hi[:, mt, :, side, :],
                               q_ps[:, m % 2, :].rearrange("p (g i) -> p g i", g=NG),
                               ACT.Copy).then_inc(q_hi_done, 1)

            def split_values(n, g):
                wait(act, c_done, NG * (n - 1) + g + 1)
                act.wait_ge(v_sum_done, NG * n + g + 1)
                act.activation(v_hi[:, g, 0:H], v_full[:, g, :], ACT.Copy).then_inc(v_hi_done, 1)

            def exponential(n, pair):
                act.wait_ge(u_sum_done, PAIRS * n + pair + 1)
                a = attn[:, 2 * pair:2 * pair + 2, :]
                act.activation(a, a, ACT.Exp, scale=SCORE_SCALE).then_inc(exp_done, 1)

            def split_weights_of_edges(n, pair):
                wait(act, c_done, NG * n)
                act.wait_ge(p_done, PAIRS * n + pair + 1)
                gs = slice(2 * pair, 2 * pair + 2)
                act.activation(p_hi[:, gs, :], attn[:, gs, :], ACT.Copy).then_inc(p_hi_done, 1)

            def copy_context(c, g):
                if isinstance(c, int) and c == 0 and g == 0:
                    act.wait_ge(w_lo_done, MATS)
                if g == 0:
                    wait(act, norm_done, NG * c)
                act.wait_ge(c_done, NG * c + g + 1)
                act.activation(c_rows[:, g, :], c_ps[:, g % 3, 0:VW], ACT.Copy).then_inc(c_copied, 1)

            def activate_turned(grp, k):
                wait(act, feat_ready[1], KT * (grp - 1) + k + 1)
                act.wait_ge(turned, KT * grp + k + 1)
                act.activation(h_full[:, k, :], c_ps[:, k, :], ACT.Relu, bias=ln_col[:, 1, k:k + 1],
                               scale=ln_col[:, 0, k:k + 1]).then_inc(h_full_done, 1)

            def split_h(grp, k):
                if k == 0:
                    if not isinstance(grp, int) or grp > 0:
                        act.wait_ge(u_done, PAIRS * (2 * grp + 1))
                act.wait_ge(h_full_done, KT * grp + k + 1)
                act.activation(feat_hi[1][:, k, :], h_full[:, k, :], ACT.Copy).then_inc(h_hi_done, 1)

            def phase(n, prev, before=(), between=()):
                if prev:
                    exponential(n - 1, 1)
                if before:
                    split_weights_of_edges(n - 1, 1)
                for job in before:
                    job()
                for m in range(QT):
                    split_queries(n, m)
                    if m == 0 and prev and not before:
                        split_weights_of_edges(n - 1, 1)
                    if between:
                        for job in between[m]:
                            job()
                for g in range(NG):
                    if prev:
                        copy_context(n - 1, g)
                    split_values(n, g)
                exponential(n, 0)
                split_weights_of_edges(n, 0)

            def relu(grp, k):
                return lambda: activate_turned(grp, k)

            def h_hi(grp, k):
                return lambda: split_h(grp, k)

            def x_hi(grp, k, scores_before):
                return lambda: split_x(grp, k, scores_before)

            def turn_first(grp):
                return [relu(grp, k) for k in range(KT)] + [h_hi(grp, k) for k in range(KT)]

            def first(t):
                if t == 0:
                    for k in range(KT):
                        split_x(0, k, 0)
                    for i in range(3):
                        split_weights(i)
                    phase(0, False, between=[[], [lambda: split_weights(3)], [], [lambda: split_weights(4)], [],
                                             [lambda: split_weights(5)]])
                    for k in range(KT):
                        split_x(1, k, PAIRS)
                else:
                    phase(1, True)
                    act.wait_ge(const_loaded, 3 * DMA)
                    phase(2, True, before=turn_first(0), between=[[], [x_hi(2, 0, 4)], [x_hi(2, 1, 4)],
                                                                  [x_hi(2, 2, 4)], [], []])

            def steady(t, b, half_t):
                n, g = 2 * t - 1, t - 1
                phase(n, True, between=[[], [], [relu(g, 0), relu(g, 1)], [relu(g, 2)], [h_hi(g, 0)],
                                        [h_hi(g, 1), h_hi(g, 2)]])
                if isinstance(t, int) and t == last:
                    phase(n + 1, True)
                else:
                    s = PAIRS * (n + 1)
                    phase(n + 1, True, between=[[], [x_hi(t + 1, 0, s)], [x_hi(t + 1, 1, s)],
                                                [x_hi(t + 1, 2, s)], [], []])

            each_turn(act, first, steady)
            end = 2 * last + 1
            phase(end, True, before=turn_first(last))
            exponential(end, 1)
            split_weights_of_edges(end, 1)
            for g in range(NG):
                copy_context(end, g)

        @block.vector
        def _(dve):
            def split_weights(i):
                dve.wait_ge(w_hi_done, i + 1)
                flat = "p a b -> p (a b)"
                hi = w_hi[:, i // 3, i % 3].rearrange(flat).bitcast(F32)
                dve.tensor_tensor(w_lo[:, i // 3, i % 3].rearrange(flat), w_stage[i], hi,
                                  ALU.subtract).then_inc(w_lo_done, 1)

            def split_queries(n, m):
                side, mt = divmod(m, KT)
                dve.wait_ge(q_hi_done, QT * n + m + 1)
                dve.tensor_tensor(q_lo[:, mt, :, side, :],
                                  q_ps[:, m % 2, :].rearrange("p (g i) -> p g i", g=NG),
                                  q_hi[:, mt, :, side, :].bitcast(F32), ALU.subtract).then_inc(q_lo_done, 1)

            def add_bias(n, l, g):
                wait(dve, v_lo_done, NG * (n - 1) + g + 1)
                dve.wait_ge(v_done, NG * n + g + 1)
                dve.tensor_tensor(v_full[:, g, :], vu_ps[:, g % 3, 0:H], bias_row[:, l, :],
                                  ALU.add).then_inc(v_sum_done, 1)

            def edge_weights(n, pair, b, mask_count):
                gs = slice(2 * pair, 2 * pair + 2)
                k = PAIRS * n + pair + 1
                if mask_count is not None:
                    dve.wait_ge(masks_ready, mask_count)
                dve.wait_ge(u_done, k)
                dve.tensor_tensor(u_masked[:, gs], vu_ps[:, 1 + pair, :].rearrange(
                    "p (g s i) -> p g s i", g=2, s=SIDES), masks[b][:, gs], ALU.mult).then_inc(masked_done, 1)
                wait(dve, p_lo_done, k - PAIRS)
                dve.wait_ge(masked_done, k)
                dve.tensor_tensor(attn[:, gs, :], u_masked[:, gs, 0, :], u_masked[:, gs, 1, :],
                                  ALU.add).then_inc(u_sum_done, 1)
                dve.wait_ge(exp_done, k)
                dve.tensor_tensor(attn[:, gs, :], attn[:, gs, :], edges[b][:, gs, 0, :],
                                  ALU.mult).then_inc(p_done, 1)

            def row_stats(c, g):
                dve.wait_ge(c_copied, NG * c + g + 1)
                dve.bn_stats(stats[:, g, :], c_rows[:, g, 0:H]).then_inc(c_stats_done, 1)

            def aggregate(c, out_grp=None):
                dve.wait_ge(c_stats_done, NG * (c + 1))
                if out_grp is not None:
                    dve.wait_ge(z_stats_done, NG * (out_grp + 1))
                dve.tensor_scalar(sum_eps[:], c_rows[:, :, H], LN_EPS, LN_EPS * SUM_EPS, ALU.mult,
                                  ALU.add).then_inc(c_aggr_done, 1)
                for g in range(NG):
                    dve.bn_aggr(mean_var[:, g, :], stats[:, g, :]).then_inc(c_aggr_done, 1)
                if out_grp is not None:
                    aggregate_out(out_grp)

            def normalise(c, dst):
                dve.wait_ge(sd_done, c + 1)
                dve.scalar_tensor_tensor(den[:], sd[:], UNBIASED, sum_eps[:], ALU.mult,
                                         ALU.add).then_inc(den_done, 1)
                dve.wait_ge(den_done, 2 * c + 1)
                dve.reciprocal(scale[:], den[:]).then_inc(den_done, 1)
                dve.wait_ge(den_done, 2 * c + 2)
                for g in range(NG):
                    dve.tensor_scalar(dst[:, g, :], c_rows[:, g, 0:H], mean_var[:, g, 0:1], scale[:, g:g + 1],
                                      ALU.subtract, ALU.mult).then_inc(norm_done, 1)

            def residual(grp, g):
                if g == 0:
                    dve.wait_ge(res_loaded, DMA * (grp + 1))
                dve.wait_ge(z_affine_done, NG * grp + g + 1)
                dve.scalar_tensor_tensor(z[:, g, :], z[:, g, :], 0.0, x_res[:, g, :], ALU.max,
                                         ALU.add).then_inc(z_res_done, 1)
                dve.wait_ge(z_res_done, NG * grp + g + 1)
                dve.bn_stats(z_stats[:, g, :], z[:, g, :]).then_inc(z_stats_done, 1)

            def aggregate_out(grp):
                for g in range(NG):
                    dve.bn_aggr(z_mean_var[:, g, :], z_stats[:, g, :]).then_inc(z_aggr_done, 1)
                dve.wait_ge(z_aggr_done, (NG + 1) * grp + NG)
                dve.tensor_scalar(z_var[:], z_mean_var[:, :, 1], OUT_EPS, None, ALU.add).then_inc(z_aggr_done, 1)

            def normalise_out(grp):
                wait(dve, stored, DMA * grp)
                dve.wait_ge(z_rstd_done, grp + 1)
                for g in range(NG):
                    dve.tensor_scalar(o_rows[:, g, :], z[:, g, :], z_mean_var[:, g, 0:1], z_rstd[:, g:g + 1],
                                      ALU.subtract, ALU.mult).then_inc(o_done, 1)

            def phase(n, l, grp, b, prev_b, prev, norm=None, out_grp=None, mask_count=None, norm_first=False):
                if prev:
                    edge_weights(n - 1, 1, prev_b, None)
                if norm_first:
                    norm()
                for m in range(QT):
                    split_queries(n, m)
                    if m == 0 and norm and not norm_first:
                        norm()
                    if out_grp is not None and m >= 3:
                        residual(out_grp, m - 3)
                if out_grp is not None:
                    residual(out_grp, 3)
                for g in range(NG):
                    add_bias(n, l, g)
                    if prev:
                        row_stats(n - 1, g)
                if prev:
                    aggregate(n - 1, out_grp)
                edge_weights(n, 0, b, mask_count)
                if out_grp is not None:
                    normalise_out(out_grp)

            def to_xhat(grp, c):
                def job():
                    wait(dve, turned, KT * grp)
                    normalise(c, xhat)
                return job

            def to_z(c):
                return lambda: normalise(c, z)

            def first(t):
                if t == 0:
                    for i in range(3):
                        split_weights(i)
                    dve.wait_ge(const_loaded, 3 * DMA)
                    for m in range(QT):
                        split_queries(0, m)
                        if m % 2:
                            split_weights(3 + m // 2)
                    for g in range(NG):
                        add_bias(0, 0, g)
                    edge_weights(0, 0, 0, 1)
                else:
                    phase(1, 0, 1, 1, 0, True, mask_count=2)
                    phase(2, 1, 0, 0, 1, True, norm=to_xhat(0, 0), norm_first=True)

            def steady(t, b, half_t):
                n = 2 * t - 1
                phase(n, 0, t, b, b, True, norm=to_xhat(t - 1, n - 2), mask_count=t + 1)
                phase(n + 1, 1, t - 1, 1 - b, b, True, norm=to_z(n - 1), out_grp=t - 2)

            each_turn(dve, first, steady)
            end = 2 * last + 1
            phase(end, 1, last, last % 2, 1 - last % 2, True, norm=to_xhat(last, end - 2), norm_first=True)
            edge_weights(end, 1, last % 2, None)
            normalise(end - 1, z)
            for g in range(NG):
                row_stats(end, g)
            for g in range(NG):
                residual(last - 1, g)
            aggregate(end, last - 1)
            normalise_out(last - 1)
            normalise(end, z)
            for g in range(NG):
                residual(last, g)
            dve.wait_ge(z_stats_done, NG * groups)
            aggregate_out(last)
            normalise_out(last)

        @block.gpsimd
        def _(pool):
            def split_x(grp, k):
                wait(pool, x_hi_done, KT * grp + k + 1)
                pool.tensor_tensor(feat_lo[0][:, k, :], x_raw[:, k, :], feat_hi[0][:, k, :].bitcast(F32),
                                   ALU.subtract).then_inc(feat_ready[0], 1)

            def split_h(grp, k):
                wait(pool, h_hi_done, KT * grp + k + 1)
                pool.tensor_tensor(feat_lo[1][:, k, :], h_full[:, k, :], feat_hi[1][:, k, :].bitcast(F32),
                                   ALU.subtract).then_inc(feat_ready[1], 1)

            def split_values(n, g):
                pool.wait_ge(v_hi_done, NG * n + g + 1)
                pool.tensor_tensor(v_lo[:, g, 0:H], v_full[:, g, :], v_hi[:, g, 0:H].bitcast(F32),
                                   ALU.subtract).then_inc(v_lo_done, 1)

            def split_weights_of_edges(n, pair):
                pool.wait_ge(p_hi_done, PAIRS * n + pair + 1)
                gs = slice(2 * pair, 2 * pair + 2)
                pool.tensor_tensor(p_lo[:, gs, :], attn[:, gs, :], p_hi[:, gs, :].bitcast(F32),
                                   ALU.subtract).then_inc(p_lo_done, 1)

            def make_masks(t, b, loads):
                if not isinstance(t, int) or t >= 2:
                    pool.wait_ge(masked_done, PAIRS * (2 * t - 1))
                wait(pool, edges_loaded[b], DMA * loads)
                pool.tensor_tensor(masks[b][:].rearrange("p g s i -> p g (s i)"),
                                   edges[b][:].rearrange("p g s i -> p g (s i)"),
                                   triangles[:].rearrange("p s i -> p (s i)").unsqueeze(1).to_broadcast(
                                       [P, NG, SIDES * P]), ALU.mult).then_inc(masks_ready, 1)

            def root(c):
                pool.wait_ge(c_aggr_done, (NG + 1) * (c + 1))
                pool.tensor_tensor(sd[:], mean_var[:, :, 1], half[:], ALU.pow).then_inc(sd_done, 1)

            def scale_and_shift(grp, c, g):
                pool.wait_ge(norm_done, NG * c + g + 1)
                pool.tensor_tensor(z[:, g, :], z[:, g, :], ln_row[:, 0, :], ALU.mult).then_inc(z_scaled, 1)
                pool.wait_ge(z_scaled, NG * grp + g + 1)
                pool.tensor_tensor(z[:, g, :], z[:, g, :], ln_row[:, 1, :], ALU.add).then_inc(z_affine_done, 1)

            def root_out(grp):
                pool.wait_ge(z_aggr_done, (NG + 1) * (grp + 1))
                pool.tensor_tensor(z_rstd[:], z_var[:], minus_half[:], ALU.pow).then_inc(z_rstd_done, 1)

            def phase(n, prev, jobs=(), out_grp=None):
                if prev:
                    split_weights_of_edges(n - 1, 1)
                for job in jobs:
                    job()
                for g in range(NG):
                    split_values(n, g)
                if prev:
                    root(n - 1)
                if out_grp is not None:
                    root_out(out_grp)
                split_weights_of_edges(n, 0)

            def h_lo(grp):
                return [lambda k=k: split_h(grp, k) for k in range(KT)]

            def x_lo(grp):
                return [lambda k=k: split_x(grp, k) for k in range(KT)]

            def first(t):
                if t == 0:
                    pool.memset(ones[:], 1.0).then_inc(blank_done, 1)
                    pool.memset(half[:], 0.5).then_inc(consts_set, 1)
                    pool.memset(minus_half[:], -0.5).then_inc(consts_set, 1)
                    pool.memset(v_lo[:, :, H:VW].bitcast(F32), 0.0).then_inc(consts_set, 1)
                    pool.memset(v_hi[:, :, H + 1:VW].bitcast(F32), 0.0).then_inc(consts_set, 1)
                    pool.memset(v_hi[:, :, H:H + 1].bitcast(F32), 1.0).then_inc(consts_set, 1)
                    pool.wait_ge(blank_done, 1)
                    pool.affine_select(out=triangles[:, 0, :], in_=ones[:], compare_op=ALU.is_ge, fill=0.0, base=0,
                                       pattern=[[-1, P]], channel_multiplier=1).then_inc(consts_set, 1)
                    pool.affine_select(out=triangles[:, 1, :], in_=ones[:], compare_op=ALU.is_gt, fill=0.0, base=0,
                                       pattern=[[1, P]], channel_multiplier=-1).then_inc(consts_set, 1)
                    pool.affine_select(out=identity[:], in_=ones[:], compare_op=ALU.is_equal, fill=0.0, base=0,
                                       pattern=[[-1, P]], channel_multiplier=1).then_inc(consts_set, 1)
                    pool.wait_ge(consts_set, CONSTS)
                    for k in range(KT):
                        split_x(0, k)
                    make_masks(0, 0, 1)
                    make_masks(1, 1, 1)
                    phase(0, False)
                    for k in range(KT):
                        split_x(1, k)
                else:
                    phase(1, True)
                    phase(2, True, h_lo(0) + x_lo(2))

            def steady(t, b, half_t):
                n = 2 * t - 1
                phase(n, True, [lambda: make_masks(t, b, half_t + 1)] + h_lo(t - 1))
                jobs = [lambda g=g: scale_and_shift(t - 2, n - 1, g) for g in range(NG)]
                if not (isinstance(t, int) and t == last):
                    jobs += x_lo(t + 1)
                phase(n + 1, True, jobs, out_grp=t - 2)

            each_turn(pool, first, steady)
            end = 2 * last + 1
            phase(end, True, h_lo(last))
            split_weights_of_edges(end, 1)
            for grp, c in ((last - 1, end - 1), (last, end)):
                for g in range(NG):
                    scale_and_shift(grp, c, g)
                if c < end:
                    root(end)
                root_out(grp)


def kernel(x, adj, L0_gnn_W_left, L0_gnn_W_right, L0_gnn_W_lin, L0_gnn_b_lin, L0_gnn_ln_a, L0_gnn_ln_b):
    import concourse.bacc as bacc
    from concourse.bass_utils import run_bass_kernel_spmd

    x, adj = np.asarray(x), np.asarray(adj)
    graphs = x.shape[0]
    groups = graphs // NG
    grouped = x.reshape(groups, NG, P, KT, P)
    a = adj.reshape(groups, NG, P, P)

    def tiles(w):
        return w.reshape(KT, P, H).transpose(1, 0, 2).reshape(P, KT * H)

    left, right, lin = (np.asarray(w) for w in (L0_gnn_W_left, L0_gnn_W_right, L0_gnn_W_lin))
    ln_a, ln_b = np.asarray(L0_gnn_ln_a), np.asarray(L0_gnn_ln_b)
    arrays = {
        "x_t": grouped.transpose(0, 4, 3, 1, 2).reshape(groups, P, KT, NODES),
        "x_rows": x,
        "edges": np.stack([a.transpose(0, 3, 1, 2), a.transpose(0, 2, 1, 3)], axis=3),
        "weights": np.stack([w for l in range(LAYERS) for w in (tiles(left[l]), tiles(right[l]), tiles(lin[l].T))]),
        "ln_cols": np.stack([ln_a[0].reshape(KT, P).T, ln_b[0].reshape(KT, P).T], axis=1),
        "ln_rows": np.stack([ln_a[1], ln_b[1]]),
        "bias_rows": np.asarray(L0_gnn_b_lin),
    }
    arrays = {name: np.ascontiguousarray(v) for name, v in arrays.items()}

    nc = bacc.Bacc("TRN2", target_bir_lowering=False, num_devices=1)
    dram = {name: nc.dram_tensor(name, v.shape, F32, kind="ExternalInput").ap() for name, v in arrays.items()}
    out = nc.dram_tensor("out", (graphs, P, H), F32, kind="ExternalOutput").ap()

    def across(ap, rows):
        return ap.rearrange("a n -> (a n)").partition_broadcast(P).rearrange("p (a n) -> p a n", a=rows)

    build_gnn(nc, dram["x_t"], dram["x_rows"].rearrange("(t g) i o -> t i g o", g=NG), dram["edges"],
              dram["weights"], dram["ln_cols"], across(dram["ln_rows"], 2), across(dram["bias_rows"], LAYERS),
              out.rearrange("(t g) i o -> t i g o", g=NG))
    result = run_bass_kernel_spmd(nc, [arrays], core_ids=[0])
    return result.results[0]["out"]
```

```python
from contextlib import ExitStack

import numpy as np

import concourse.bass as bass
from concourse import mybir

F32 = mybir.dt.float32
F32R = mybir.dt.float32r
ALU = mybir.AluOpType
ACT = mybir.ActivationFunctionType

P = 128
H = 384
KT = H // P
LAYERS = 2
NG = 4
NODES = NG * P
SIDES = 2
QT = SIDES * KT
PAIRS = NG // 2
VW = H + 2
BANK = 512
DMA = 16
LN_EPS = 1e-3
SUM_EPS = 1e-10
OUT_EPS = 1e-5
UNBIASED = float(np.sqrt(H / (H - 1.0)))
SCORE_SCALE = 1.0 / float(np.sqrt(H))


def build_gnn(nc, x_t, x_rows, edges_dram, weights, ln_cols, ln_rows, bias_rows, out):
    groups = x_t.shape[0]
    last = groups - 1

    with ExitStack() as ctx:
        def sb(name, shape, dt=F32):
            return ctx.enter_context(nc.sbuf_tensor(name, shape, dt))

        def sem(name):
            return ctx.enter_context(nc.semaphore(name))

        w_hi = sb("w_hi", [P, LAYERS, 3, KT, H], F32R)
        w_lo = sb("w_lo", [P, LAYERS, 3, KT, H], F32R)
        x_raw = sb("x_raw", [P, KT, NODES])
        feat_hi = [sb(f"feat_hi{f}", [P, KT, NODES], F32R) for f in range(2)]
        feat_lo = [sb(f"feat_lo{f}", [P, KT, NODES], F32R) for f in range(2)]
        h_full = sb("h_full", [P, KT, NODES])
        q_hi = sb("q_hi", [P, KT, NG, SIDES, P], F32R)
        q_lo = sb("q_lo", [P, KT, NG, SIDES, P], F32R)
        v_full = sb("v_full", [P, NG, H])
        v_hi = sb("v_hi", [P, NG, VW], F32R)
        v_lo = sb("v_lo", [P, NG, VW], F32R)
        edges = [sb(f"edges{b}", [P, NG, 2, P]) for b in range(2)]
        masks = [sb(f"masks{b}", [P, NG, SIDES, P]) for b in range(2)]
        u_masked = sb("u_masked", [P, NG, SIDES, P])
        attn = sb("attn", [P, NG, P])
        p_hi = sb("p_hi", [P, NG, P], F32R)
        p_lo = sb("p_lo", [P, NG, P], F32R)
        c_rows = sb("c_rows", [P, NG, VW])
        xhat = sb("xhat", [P, NG, H])
        z = sb("z", [P, NG, H])
        x_res = sb("x_res", [P, NG, H])
        o_rows = sb("o_rows", [P, NG, H])
        identity = sb("identity", [P, P])
        ones = sb("ones", [P, P])
        triangles = sb("triangles", [P, SIDES, P])
        half = sb("half", [P, NG])
        minus_half = sb("minus_half", [P, NG])
        ln_col = sb("ln_col", [P, 2, KT])
        ln_row = sb("ln_row", [P, 2, H])
        bias_row = sb("bias_row", [P, LAYERS, H])
        stats = sb("stats", [P, NG, 6])
        mean_var = sb("mean_var", [P, NG, 2])
        sum_eps = sb("sum_eps", [P, NG])
        sd = sb("sd", [P, NG])
        den = sb("den", [P, NG])
        scale = sb("scale", [P, NG])
        z_stats = sb("z_stats", [P, NG, 6])
        z_mean_var = sb("z_mean_var", [P, NG, 2])
        z_var = sb("z_var", [P, NG])
        z_rstd = sb("z_rstd", [P, NG])
        norm_bias = sb("norm_bias", [P, NG])
        out_bias = sb("out_bias", [P, NG])

        def staging(buffer):
            return buffer.rearrange("p a b -> p (a b)")[:, 0:KT * H]

        w_stage = [staging(b) for b in (xhat[:], z[:], o_rows[:], x_res[:], c_rows[:], h_full[:])]
        MATS = len(w_stage)

        q_ps = ctx.enter_context(nc.psum_tensor("q_ps", [P, 2, BANK], F32))
        vu_ps = ctx.enter_context(nc.psum_tensor("vu_ps", [P, 3, BANK], F32))
        c_ps = ctx.enter_context(nc.psum_tensor("c_ps", [P, 3, BANK], F32))

        o_end = c_rows[:, :, 0:H]
        c_end = (c_ps, q_ps)

        w_loaded = [sem(f"w_loaded{i}") for i in range(1, MATS)]
        w_first_loaded = [sem(f"w_first_loaded{k}") for k in range(KT)]
        x_first_loaded = [sem(f"x_first_loaded{k}") for k in range(KT)]
        x_loaded = sem("x_loaded")
        const_loaded = sem("const_loaded")
        edges_loaded = [sem(f"edges_loaded{b}") for b in range(2)]
        res_loaded = sem("res_loaded")
        stored = sem("stored")
        q_done = sem("q_done")
        v_done = sem("v_done")
        u_done = sem("u_done")
        c_done = sem("c_done")
        turned = sem("turned")
        w_first_hi_done = sem("w_first_hi_done")
        w_first_ready = sem("w_first_ready")
        w_hi_done = sem("w_hi_done")
        w_lo_done = sem("w_lo_done")
        x_hi_done = sem("x_hi_done")
        feat_ready = [sem(f"feat_ready{l}") for l in range(LAYERS)]
        h_full_done = sem("h_full_done")
        h_hi_done = sem("h_hi_done")
        q_hi_done = sem("q_hi_done")
        q_lo_done = sem("q_lo_done")
        v_sum_done = sem("v_sum_done")
        v_hi_done = sem("v_hi_done")
        v_lo_done = sem("v_lo_done")
        masked_done = sem("masked_done")
        u_sum_done = sem("u_sum_done")
        exp_done = sem("exp_done")
        p_done = sem("p_done")
        p_hi_done = sem("p_hi_done")
        p_lo_done = sem("p_lo_done")
        masks_ready = sem("masks_ready")
        c_copied = sem("c_copied")
        c_stats_done = sem("c_stats_done")
        c_aggr_done = sem("c_aggr_done")
        sd_done = sem("sd_done")
        den_done = sem("den_done")
        norm_done = sem("norm_done")
        z_scaled = sem("z_scaled")
        z_affine_done = sem("z_affine_done")
        z_res_done = sem("z_res_done")
        z_stats_done = sem("z_stats_done")
        z_aggr_done = sem("z_aggr_done")
        z_rstd_done = sem("z_rstd_done")
        o_done = sem("o_done")
        z_shift_done = sem("z_shift_done")
        end_stats_done = sem("end_stats_done")
        end_aggr_done = sem("end_aggr_done")
        end_sd_done = sem("end_sd_done")
        end_scale_done = sem("end_scale_done")
        end_centred = sem("end_centred")
        end_norm_done = sem("end_norm_done")
        end_var_done = sem("end_var_done")
        end_rstd_done = sem("end_rstd_done")
        out_bias_done = sem("out_bias_done")
        end_out_done = [sem(f"end_out_done{pair}") for pair in range(PAIRS)]
        consts_set = sem("consts_set")
        blank_done = sem("blank_done")

        CONSTS = 8

        def wait(eng, semaphore, value):
            if not isinstance(value, int) or value > 0:
                eng.wait_ge(semaphore, value)

        def nodes(g):
            return slice(g * P, (g + 1) * P)

        def each_turn(eng, first, steady):
            first(0)
            first(1)
            with eng.Fori(1, groups // 2 - 1) as pair:
                for b in range(2):
                    steady(2 * pair + b, b, pair)
            for t in (last - 1, last):
                steady(t, t % 2, t // 2)

        block = ctx.enter_context(nc.Block())

        @block.sync
        def _(sp):
            def load_edges(t, b):
                if not isinstance(t, int) or t >= 2:
                    wait(sp, p_done, PAIRS * (2 * t - 1))
                sp.dma_start(edges[b][:], edges_dram[t]).then_inc(edges_loaded[b], DMA)

            def load_x(g):
                wait(sp, feat_ready[0], KT * g)
                sp.dma_start(x_raw[:], x_t[g]).then_inc(x_loaded, DMA)

            def load_res(g):
                wait(sp, z_res_done, NG * g)
                sp.dma_start(x_res[:], x_rows[g]).then_inc(res_loaded, DMA)

            def store(g):
                wait(sp, o_done, NG * (g + 1))
                sp.dma_start(out[g], o_rows[:]).then_inc(stored, DMA)

            def load_weights(i):
                sp.dma_start(w_stage[i], weights[i]).then_inc(w_loaded[i - 1], DMA)

            for k in range(KT):
                sp.dma_start(x_raw[:, k, :], x_t[0][:, k, :]).then_inc(x_first_loaded[k], DMA)
                sp.dma_start(w_stage[0][:, k * H:(k + 1) * H],
                             weights[0][:, k * H:(k + 1) * H]).then_inc(w_first_loaded[k], DMA)
            load_weights(1)
            load_weights(2)
            load_edges(0, 0)
            sp.dma_start(bias_row[:], bias_rows).then_inc(const_loaded, DMA)
            sp.dma_start(ln_col[:], ln_cols).then_inc(const_loaded, DMA)
            sp.dma_start(ln_row[:], ln_rows).then_inc(const_loaded, DMA)
            for i in range(3, MATS):
                load_weights(i)
            load_x(1)
            load_edges(1, 1)

            def first(t):
                if t == 1:
                    load_x(2)
                    sp.wait_ge(w_lo_done, MATS - 1)

            def steady(t, b, half_t):
                load_edges(t, b)
                load_res(t - 2)
                if not (isinstance(t, int) and t == last):
                    load_x(t + 1)
                store(t - 2)

            each_turn(sp, first, steady)
            load_res(last - 1)
            load_res(last)
            store(last - 1)
            for pair in range(PAIRS):
                gs = slice(2 * pair, 2 * pair + 2)
                sp.wait_ge(end_out_done[pair], 2)
                sp.dma_start(out[last][:, gs], o_end[:, gs]).then_inc(stored, DMA)
            sp.wait_ge(stored, DMA * (last + PAIRS))

        @block.tensor
        def _(pe):
            def product(out_ap, left, right, start, stop):
                (l_hi, l_lo), (r_hi, r_lo) = left, right
                pe.matmul(out_ap, l_hi, r_hi, start=start, stop=False)
                pe.matmul(out_ap, l_hi, r_lo, start=False, stop=False)
                return pe.matmul(out_ap, l_lo, r_hi, start=False, stop=stop)

            def queries(n, l, f, grp, m):
                wait(pe, q_lo_done, QT * n + m - 1)
                side, mt = divmod(m, KT)
                for k in range(KT):
                    if m == 0:
                        wait(pe, feat_ready[l], KT * grp + k + 1)
                    if isinstance(n, int) and n == 0 and m == 0:
                        pe.wait_ge(w_first_ready, k + 1)
                    elif isinstance(n, int) and n in (0, 2) and mt == 0 and k == 0:
                        pe.wait_ge(w_lo_done, 3 * l + side)
                    cols = slice(mt * P, (mt + 1) * P)
                    mm = product(q_ps[:, m % 2, :],
                                 (w_hi[:, l, side, k, cols], w_lo[:, l, side, k, cols]),
                                 (feat_hi[f][:, k, :], feat_lo[f][:, k, :]), k == 0, k == KT - 1)
                mm.then_inc(q_done, 1)

            def values(n, l, f, g):
                if g == 0:
                    wait(pe, v_sum_done, NG * n)
                elif g == 3:
                    pe.wait_ge(v_sum_done, NG * n + 1)
                else:
                    wait(pe, masked_done, PAIRS * n + g - 2)
                if isinstance(n, int) and n in (0, 2) and g == 0:
                    pe.wait_ge(w_lo_done, 3 * l + 2)
                for k in range(KT):
                    mm = product(vu_ps[:, g % 3, 0:H],
                                 (feat_hi[f][:, k, nodes(g)], feat_lo[f][:, k, nodes(g)]),
                                 (w_hi[:, l, 2, k, :], w_lo[:, l, 2, k, :]), k == 0, k == KT - 1)
                mm.then_inc(v_done, 1)

            def scores(n, f, pair):
                if pair == 0:
                    pe.wait_ge(q_lo_done, QT * (n + 1))
                pe.wait_ge(v_sum_done, NG * n + 2 + pair)
                for g in (2 * pair, 2 * pair + 1):
                    at = (g % 2) * SIDES * P
                    for k in range(KT):
                        mm = product(vu_ps[:, 1 + pair, at:at + SIDES * P],
                                     (feat_hi[f][:, k, nodes(g)], feat_lo[f][:, k, nodes(g)]),
                                     (q_hi[:, k, g], q_lo[:, k, g]), k == 0, k == KT - 1)
                mm.then_inc(u_done, 1)

            def context(c, g, turned_groups):
                if g == 0:
                    wait(pe, c_copied, NG * c)
                    wait(pe, h_full_done, KT * turned_groups)
                if g == 3:
                    pe.wait_ge(c_copied, NG * c + 1)
                if g % 2 == 0:
                    pe.wait_ge(p_lo_done, PAIRS * c + g // 2 + 1)
                pe.wait_ge(v_lo_done, NG * c + g + 1)
                product(c_ps[:, g % 3, 0:VW], (p_hi[:, g, :], p_lo[:, g, :]),
                        (v_hi[:, g, :], v_lo[:, g, :]), True, True).then_inc(c_done, 1)

            def turn(grp, contexts):
                pe.wait_ge(c_copied, NG * contexts)
                pe.wait_ge(norm_done, NG * contexts)
                for k in range(KT):
                    for g in range(NG):
                        tr = pe.transpose(c_ps[:, k, nodes(g)], xhat[:, g, k * P:(k + 1) * P], identity[:])
                    tr.then_inc(turned, 1)

            def phase(n, l, f, grp, prev, turned_groups, turn_mid=None, early=False, turn_late=None):
                for m in range(QT):
                    if m == 3 and early:
                        for g in range(NG):
                            context(n - 1, g, turned_groups)
                    if m == 4 and turn_mid:
                        turn(*turn_mid)
                    queries(n, l, f, grp, m)
                for g in range(NG):
                    if g == 2 and turn_late:
                        turn(*turn_late)
                    if prev and not early:
                        context(n - 1, g, turned_groups)
                    values(n, l, f, g)
                for pair in range(PAIRS):
                    scores(n, f, pair)

            def first(t):
                if t == 0:
                    pe.wait_ge(consts_set, CONSTS)
                    phase(0, 0, 0, 0, False, 0)
                else:
                    phase(1, 0, 1, 1, True, 0, early=True, turn_late=(0, 1))
                    phase(2, 1, 0, 0, True, 1)

            def steady(t, b, half_t):
                n = 2 * t - 1
                phase(n, 0, 1, t, True, t, turn_mid=(t - 1, n - 1))
                if isinstance(t, int) and t == last:
                    phase(n + 1, 1, 0, t - 1, True, t, early=True, turn_late=(last, n + 1))
                else:
                    phase(n + 1, 1, 0, t - 1, True, t)

            each_turn(pe, first, steady)
            end = 2 * last + 1
            phase(end, 1, 1, last, True, groups, early=True)
            for g in range(NG):
                if g == 0:
                    pe.wait_ge(c_copied, NG * end)
                if g % 2 == 0:
                    pe.wait_ge(p_lo_done, PAIRS * end + g // 2 + 1)
                if g == 2:
                    pe.wait_ge(q_lo_done, QT * (end + 1))
                pe.wait_ge(v_lo_done, NG * end + g + 1)
                product(c_end[g // 2][:, g % 2, 0:VW], (p_hi[:, g, :], p_lo[:, g, :]),
                        (v_hi[:, g, :], v_lo[:, g, :]), True, True).then_inc(c_done, 1)

        @block.scalar
        def _(act):
            def split_weights(i):
                act.wait_ge(w_loaded[i - 1], DMA)
                act.activation(w_hi[:, i // 3, i % 3].rearrange("p a b -> p (a b)"), w_stage[i],
                               ACT.Copy).then_inc(w_hi_done, 1)

            def split_first(k):
                act.wait_ge(x_first_loaded[k], DMA)
                act.activation(feat_hi[0][:, k, :], x_raw[:, k, :], ACT.Copy).then_inc(x_hi_done, 1)
                act.wait_ge(w_first_loaded[k], DMA)
                act.activation(w_hi[:, 0, 0, k], w_stage[0][:, k * H:(k + 1) * H],
                               ACT.Copy).then_inc(w_first_hi_done, 1)

            def split_x(grp, k):
                if k == 0:
                    wait(act, x_loaded, DMA * grp)
                    if not isinstance(grp, int) or grp > 1:
                        act.wait_ge(u_done, PAIRS * (2 * grp - 2))
                act.activation(feat_hi[1][:, k, :], x_raw[:, k, :], ACT.Copy).then_inc(x_hi_done, 1)

            def split_queries(n, m):
                side, mt = divmod(m, KT)
                if m == 0:
                    wait(act, u_done, PAIRS * n)
                act.wait_ge(q_done, QT * n + m + 1)
                act.activation(q_hi[:, mt, :, side, :],
                               q_ps[:, m % 2, :].rearrange("p (g i) -> p g i", g=NG),
                               ACT.Copy).then_inc(q_hi_done, 1)

            def split_values(n, g):
                wait(act, c_done, NG * (n - 1) + g + 1)
                act.wait_ge(v_sum_done, NG * n + g + 1)
                act.activation(v_hi[:, g, 0:H], v_full[:, g, :], ACT.Copy).then_inc(v_hi_done, 1)

            def exponential(n, pair):
                act.wait_ge(u_sum_done, PAIRS * n + pair + 1)
                a = attn[:, 2 * pair:2 * pair + 2, :]
                act.activation(a, a, ACT.Exp, scale=SCORE_SCALE).then_inc(exp_done, 1)

            def split_weights_of_edges(n, pair):
                wait(act, c_done, NG * n)
                act.wait_ge(p_done, PAIRS * n + pair + 1)
                gs = slice(2 * pair, 2 * pair + 2)
                act.activation(p_hi[:, gs, :], attn[:, gs, :], ACT.Copy).then_inc(p_hi_done, 1)

            def copy_context(c, g):
                if isinstance(c, int) and c == 0 and g == 0:
                    act.wait_ge(w_lo_done, MATS - 1)
                if g == 0:
                    wait(act, norm_done, NG * c)
                act.wait_ge(c_done, NG * c + g + 1)
                act.activation(c_rows[:, g, :], c_ps[:, g % 3, 0:VW], ACT.Copy).then_inc(c_copied, 1)

            def activate_turned(grp, k):
                wait(act, feat_ready[1], KT * (grp - 1) + k + 1)
                act.wait_ge(turned, KT * grp + k + 1)
                act.activation(h_full[:, k, :], c_ps[:, k, :], ACT.Relu, bias=ln_col[:, 1, k:k + 1],
                               scale=ln_col[:, 0, k:k + 1]).then_inc(h_full_done, 1)

            def split_h(grp, k, f=0):
                if k == 0:
                    act.wait_ge(u_done, PAIRS * (2 * grp + 1 if f == 0 else 2 * grp))
                act.wait_ge(h_full_done, KT * grp + k + 1)
                act.activation(feat_hi[f][:, k, :], h_full[:, k, :], ACT.Copy).then_inc(h_hi_done, 1)

            def phase(n, prev, after=None, early=False, late=()):
                for m in range(QT):
                    split_queries(n, m)
                    if prev and m == 0:
                        exponential(n - 1, 1)
                        split_weights_of_edges(n - 1, 1)
                    if early and m == 2:
                        for g in range(NG):
                            copy_context(n - 1, g)
                    for job in after[m] if after else ():
                        job()
                for g in range(NG):
                    if prev and not early:
                        copy_context(n - 1, g)
                    if g == 2:
                        for job in late:
                            job()
                    split_values(n, g)
                exponential(n, 0)
                split_weights_of_edges(n, 0)

            def relu(grp, k):
                return lambda: activate_turned(grp, k)

            def h_hi(grp, k):
                return lambda: split_h(grp, k)

            def x_hi(grp):
                return [[], *([lambda k=k: split_x(grp, k)] for k in range(KT)), [], []]

            def turn_late(grp, f):
                return [relu(grp, k) for k in range(KT)] + [lambda k=k: split_h(grp, k, f) for k in range(KT)]

            def first(t):
                if t == 0:
                    for k in range(KT):
                        split_first(k)
                    w1, w2, w3, w4, w5 = ([lambda i=i: split_weights(i)] for i in range(1, MATS))
                    phase(0, False, [w1, w2, [], w3, w4, w5], late=[lambda k=k: split_x(1, k) for k in range(KT)])
                else:
                    act.wait_ge(const_loaded, 3 * DMA)
                    phase(1, True, early=True, late=turn_late(0, 0))
                    phase(2, True, x_hi(2))

            def steady(t, b, half_t):
                n, g = 2 * t - 1, t - 1
                phase(n, True, [[], [], [], [relu(g, 0), relu(g, 1)], [relu(g, 2)], [h_hi(g, k) for k in range(KT)]])
                if isinstance(t, int) and t == last:
                    phase(n + 1, True, early=True, late=turn_late(last, 1))
                else:
                    phase(n + 1, True, x_hi(t + 1))

            each_turn(act, first, steady)
            end = 2 * last + 1
            phase(end, True, early=True)
            exponential(end, 1)
            split_weights_of_edges(end, 1)

            act.wait_ge(turned, KT * groups)
            for pair in range(PAIRS):
                g = 2 * pair + 1
                act.wait_ge(end_scale_done, 3 * (pair + 1))
                act.activation(xhat[:, g, :], c_end[pair][:, 1, 0:H], ACT.Identity, bias=norm_bias[:, g:g + 1],
                               scale=scale[:, g:g + 1]).then_inc(end_norm_done, 1)
            act.wait_ge(out_bias_done, 1)
            act.wait_ge(stored, DMA * (last - 1))
            for g in range(NG):
                act.activation(o_rows[:, g, :], z[:, g, :], ACT.Identity, bias=out_bias[:, g:g + 1],
                               scale=z_rstd[:, g:g + 1]).then_inc(o_done, 1)
            act.wait_ge(norm_done, NG * end)
            for pair in range(PAIRS):
                g = 2 * pair + 1
                act.wait_ge(out_bias_done, 1 + pair + 1)
                act.activation(o_end[:, g, :], xhat[:, g, :], ACT.Identity, bias=out_bias[:, g:g + 1],
                               scale=z_rstd[:, g:g + 1]).then_inc(end_out_done[pair], 1)

        @block.vector
        def _(dve):
            def split_first(k):
                dve.wait_ge(x_hi_done, k + 1)
                dve.tensor_tensor(feat_lo[0][:, k, :], x_raw[:, k, :], feat_hi[0][:, k, :].bitcast(F32),
                                  ALU.subtract).then_inc(feat_ready[0], 1)
                dve.wait_ge(w_first_hi_done, k + 1)
                dve.tensor_tensor(w_lo[:, 0, 0, k], w_stage[0][:, k * H:(k + 1) * H],
                                  w_hi[:, 0, 0, k].bitcast(F32), ALU.subtract).then_inc(w_first_ready, 1)

            def split_weights(i):
                dve.wait_ge(w_hi_done, i)
                flat = "p a b -> p (a b)"
                hi = w_hi[:, i // 3, i % 3].rearrange(flat).bitcast(F32)
                dve.tensor_tensor(w_lo[:, i // 3, i % 3].rearrange(flat), w_stage[i], hi,
                                  ALU.subtract).then_inc(w_lo_done, 1)

            def split_queries(n, m):
                side, mt = divmod(m, KT)
                dve.wait_ge(q_hi_done, QT * n + m + 1)
                dve.tensor_tensor(q_lo[:, mt, :, side, :],
                                  q_ps[:, m % 2, :].rearrange("p (g i) -> p g i", g=NG),
                                  q_hi[:, mt, :, side, :].bitcast(F32), ALU.subtract).then_inc(q_lo_done, 1)

            def add_bias(n, l, g):
                wait(dve, v_lo_done, NG * (n - 1) + g + 1)
                dve.wait_ge(v_done, NG * n + g + 1)
                dve.tensor_tensor(v_full[:, g, :], vu_ps[:, g % 3, 0:H], bias_row[:, l, :],
                                  ALU.add).then_inc(v_sum_done, 1)

            def mask_scores(n, pair, b, mask_count=None):
                gs = slice(2 * pair, 2 * pair + 2)
                k = PAIRS * n + pair + 1
                if mask_count is not None:
                    dve.wait_ge(masks_ready, mask_count)
                dve.wait_ge(u_done, k)
                dve.tensor_tensor(u_masked[:, gs], vu_ps[:, 1 + pair, :].rearrange(
                    "p (g s i) -> p g s i", g=2, s=SIDES), masks[b][:, gs], ALU.mult).then_inc(masked_done, 1)
                wait(dve, p_lo_done, k - PAIRS)
                dve.wait_ge(masked_done, k)
                dve.tensor_tensor(attn[:, gs, :], u_masked[:, gs, 0, :], u_masked[:, gs, 1, :],
                                  ALU.add).then_inc(u_sum_done, 1)

            def weigh(n, pair, b):
                gs = slice(2 * pair, 2 * pair + 2)
                dve.wait_ge(exp_done, PAIRS * n + pair + 1)
                dve.tensor_tensor(attn[:, gs, :], attn[:, gs, :], edges[b][:, gs, 0, :],
                                  ALU.mult).then_inc(p_done, 1)

            def row_stats(c, g):
                dve.wait_ge(c_copied, NG * c + g + 1)
                dve.bn_stats(stats[:, g, :], c_rows[:, g, 0:H]).then_inc(c_stats_done, 1)

            def aggregate(c, out_grp=None):
                dve.wait_ge(c_stats_done, NG * (c + 1))
                if out_grp is not None:
                    dve.wait_ge(z_stats_done, NG * (out_grp + 1))
                dve.tensor_scalar(sum_eps[:], c_rows[:, :, H], LN_EPS, LN_EPS * SUM_EPS, ALU.mult,
                                  ALU.add).then_inc(c_aggr_done, 1)
                for g in range(NG):
                    dve.bn_aggr(mean_var[:, g, :], stats[:, g, :]).then_inc(c_aggr_done, 1)
                if out_grp is not None:
                    aggregate_out(out_grp)

            def norm_scale(c):
                dve.wait_ge(sd_done, c + 1)
                dve.scalar_tensor_tensor(den[:], sd[:], UNBIASED, sum_eps[:], ALU.mult,
                                         ALU.add).then_inc(den_done, 1)
                dve.wait_ge(den_done, 2 * c + 1)
                dve.reciprocal(scale[:], den[:]).then_inc(den_done, 1)
                dve.wait_ge(den_done, 2 * c + 2)

            def normalise(dst, g):
                dve.tensor_scalar(dst[:, g, :], c_rows[:, g, 0:H], mean_var[:, g, 0:1], scale[:, g:g + 1],
                                  ALU.subtract, ALU.mult).then_inc(norm_done, 1)

            def add_row(grp, g):
                dve.scalar_tensor_tensor(z[:, g, :], z[:, g, :], 0.0, x_res[:, g, :], ALU.max,
                                         ALU.add).then_inc(z_res_done, 1)

            def out_stats(grp, g):
                dve.bn_stats(z_stats[:, g, :], z[:, g, :]).then_inc(z_stats_done, 1)

            def residual(grp, g):
                if g == 0:
                    dve.wait_ge(res_loaded, DMA * (grp + 1))
                dve.wait_ge(z_affine_done, NG * grp + g + 1)
                add_row(grp, g)
                dve.wait_ge(z_res_done, NG * grp + g + 1)
                out_stats(grp, g)

            def aggregate_out(grp):
                for g in range(NG):
                    dve.bn_aggr(z_mean_var[:, g, :], z_stats[:, g, :]).then_inc(z_aggr_done, 1)
                dve.wait_ge(z_aggr_done, (NG + 1) * grp + NG)
                dve.tensor_scalar(z_var[:], z_mean_var[:, :, 1], OUT_EPS, None, ALU.add).then_inc(z_aggr_done, 1)

            def normalise_out(grp):
                wait(dve, stored, DMA * grp)
                dve.wait_ge(z_rstd_done, grp + 1)
                for g in range(NG):
                    dve.tensor_scalar(o_rows[:, g, :], z[:, g, :], z_mean_var[:, g, 0:1], z_rstd[:, g:g + 1],
                                      ALU.subtract, ALU.mult).then_inc(o_done, 1)

            def phase(n, l, b, prev_b, prev, after=None, early=False, out_grp=None, mask_count=None,
                      between=(), masked=()):
                if prev:
                    mask_scores(n - 1, 1, prev_b)
                for m in range(QT):
                    split_queries(n, m)
                    if prev and m == 0:
                        weigh(n - 1, 1, prev_b)
                    for job in after[m] if after else ():
                        job()
                for g in range(NG):
                    add_bias(n, l, g)
                    if prev and not early:
                        row_stats(n - 1, g)
                    if g < len(between):
                        between[g]()
                if prev and not early:
                    aggregate(n - 1, out_grp)
                mask_scores(n, 0, b, mask_count)
                for job in masked:
                    job()
                weigh(n, 0, b)

            def to_rows(c, dst, turned_before=None):
                def one():
                    if turned_before is not None:
                        wait(dve, turned, turned_before)
                    norm_scale(c)
                    normalise(dst, 0)
                    normalise(dst, 1)

                def two():
                    normalise(dst, 2)
                    normalise(dst, 3)
                return one, two

            def early_stats(c):
                def job():
                    for g in range(NG):
                        row_stats(c, g)
                    aggregate(c)
                return job

            def add_residual(grp, *gs):
                return lambda: [residual(grp, g) for g in gs]

            def centre(g):
                dve.scalar_tensor_tensor(z[:, g, :], c_rows[:, g, 0:H], mean_var[:, g, 0:1], ln_row[:, 0, :],
                                         ALU.subtract, ALU.mult).then_inc(norm_done, 1)

            def shift(g):
                dve.scalar_tensor_tensor(z[:, g, :], z[:, g, :], scale[:, g:g + 1], ln_row[:, 1, :],
                                         ALU.mult, ALU.add).then_inc(z_shift_done, 1)

            def first(t):
                if t == 0:
                    for k in range(KT):
                        split_first(k)
                    w1, w2, w3, w4, w5 = ([lambda i=i: split_weights(i)] for i in range(1, MATS))
                    rows_loaded = [lambda: dve.wait_ge(const_loaded, 3 * DMA)]
                    phase(0, 0, 0, 0, False, [w1, w2, [], w3, w4, w5 + rows_loaded], mask_count=1)
                else:
                    one, two = to_rows(0, xhat)
                    phase(1, 0, 1, 0, True, [[], [], [early_stats(0)], [], [one], [two]], early=True, mask_count=2)
                    phase(2, 1, 0, 1, True)

            def steady(t, b, half_t):
                n = 2 * t - 1
                one, two = to_rows(n - 2, xhat, KT * (t - 1))
                phase(n, 0, b, b, True, [[one], [two], [], [], [], []], mask_count=t + 1)
                one, two = to_rows(n - 1, z)
                if isinstance(t, int) and t == last:
                    x_one, x_two = to_rows(n, xhat, KT * last)
                    phase(n + 1, 1, 1 - b, b, True,
                          [[one], [two], [early_stats(n)], [add_residual(t - 2, 0)], [add_residual(t - 2, 1)],
                           [x_one, x_two, add_residual(t - 2, 2, 3)]], early=True)
                    dve.wait_ge(z_stats_done, NG * (t - 1))
                    aggregate_out(t - 2)
                else:
                    phase(n + 1, 1, 1 - b, b, True,
                          [[one], [two], [], [add_residual(t - 2, 0)], [add_residual(t - 2, 1)],
                           [add_residual(t - 2, 2, 3)]], out_grp=t - 2)
                    normalise_out(t - 2)

            each_turn(dve, first, steady)
            end = 2 * last + 1

            def next_to_last_rows():
                norm_scale(end - 1)
                normalise(z, 2)
                normalise(z, 3)
                centre(0)

            def next_to_last_centre():
                centre(1)
                dve.wait_ge(norm_done, NG * end)
                shift(0)

            def next_to_last_residual():
                shift(1)
                dve.wait_ge(z_shift_done, 2)
                dve.wait_ge(res_loaded, DMA * last)
                add_row(last - 1, 0)

            def next_to_last_stats():
                add_row(last - 1, 1)
                dve.wait_ge(z_res_done, NG * (last - 1) + 2)
                out_stats(last - 1, 0)

            def next_to_last_rest():
                out_stats(last - 1, 1)
                dve.wait_ge(z_affine_done, NG * (last - 1) + 2)
                add_row(last - 1, 2)

            phase(end, 1, last % 2, 1 - last % 2, True,
                  [[], [lambda: normalise_out(last - 2)], [early_stats(end - 1)], [],
                   [next_to_last_rows], [next_to_last_centre]], early=True,
                  between=[next_to_last_residual, next_to_last_stats, next_to_last_rest],
                  masked=[lambda: add_row(last - 1, 3)])
            mask_scores(end, 1, last % 2)
            dve.wait_ge(z_res_done, NG * last)
            out_stats(last - 1, 2)
            weigh(end, 1, last % 2)
            out_stats(last - 1, 3)
            dve.wait_ge(z_stats_done, NG * last)
            aggregate_out(last - 1)

            def pair_stats(pair):
                gs, c = slice(2 * pair, 2 * pair + 2), c_end[pair]
                for i in range(2):
                    dve.wait_ge(c_done, NG * end + 2 * pair + i + 1)
                    dve.bn_stats(stats[:, 2 * pair + i, :], c[:, i, 0:H]).then_inc(end_stats_done, 1)
                dve.tensor_scalar(sum_eps[:, gs], c[:, 0:2, H], LN_EPS, LN_EPS * SUM_EPS, ALU.mult,
                                  ALU.add).then_inc(end_aggr_done, 1)
                dve.wait_ge(end_stats_done, 2 * pair + 2)
                for g in (2 * pair, 2 * pair + 1):
                    dve.bn_aggr(mean_var[:, g, :], stats[:, g, :]).then_inc(end_aggr_done, 1)

            def pair_scale(pair):
                gs = slice(2 * pair, 2 * pair + 2)
                dve.wait_ge(end_sd_done, pair + 1)
                dve.scalar_tensor_tensor(den[:, gs], sd[:, gs], UNBIASED, sum_eps[:, gs], ALU.mult,
                                         ALU.add).then_inc(end_scale_done, 1)
                dve.wait_ge(end_scale_done, 3 * pair + 1)
                dve.reciprocal(scale[:, gs], den[:, gs]).then_inc(end_scale_done, 1)
                dve.wait_ge(end_scale_done, 3 * pair + 2)
                dve.scalar_tensor_tensor(norm_bias[:, gs], mean_var[:, gs, 0], -1.0, scale[:, gs], ALU.mult,
                                         ALU.mult).then_inc(end_scale_done, 1)

            def pair_rows(pair):
                g = 2 * pair
                dve.scalar_tensor_tensor(xhat[:, g, :], c_end[pair][:, 0, 0:H], mean_var[:, g, 0:1], ln_row[:, 0, :],
                                         ALU.subtract, ALU.mult).then_inc(end_centred, 1)
                dve.wait_ge(end_centred, pair + 1)
                dve.scalar_tensor_tensor(xhat[:, g, :], xhat[:, g, :], scale[:, g:g + 1], ln_row[:, 1, :],
                                         ALU.mult, ALU.add).then_inc(z_shift_done, 1)

            def add_end_row(g):
                dve.scalar_tensor_tensor(xhat[:, g, :], xhat[:, g, :], 0.0, x_res[:, g, :], ALU.max,
                                         ALU.add).then_inc(z_res_done, 1)

            def pair_own_residual(pair):
                dve.wait_ge(z_shift_done, 2 + pair + 1)
                if pair == 0:
                    dve.wait_ge(res_loaded, DMA * groups)
                add_end_row(2 * pair)

            def pair_out_stats(pair, added):
                g = 2 * pair
                dve.wait_ge(z_affine_done, NG * last + pair - 2 + 1)
                add_end_row(g + 1)
                dve.wait_ge(z_res_done, NG * last + added - 1)
                dve.bn_stats(z_stats[:, g, :], xhat[:, g, :]).then_inc(z_stats_done, 1)
                dve.wait_ge(z_res_done, NG * last + added)
                dve.bn_stats(z_stats[:, g + 1, :], xhat[:, g + 1, :]).then_inc(z_stats_done, 1)
                dve.wait_ge(z_stats_done, NG * last + g + 2)
                for i in (g, g + 1):
                    dve.bn_aggr(z_mean_var[:, i, :], z_stats[:, i, :]).then_inc(end_var_done, 1)
                dve.wait_ge(end_var_done, 3 * pair + 2)
                dve.tensor_scalar(z_var[:, g:g + 2], z_mean_var[:, g:g + 2, 1], OUT_EPS, None,
                                  ALU.add).then_inc(end_var_done, 1)

            def negative_out_means(gs):
                dve.scalar_tensor_tensor(out_bias[:, gs], z_mean_var[:, gs, 0], -1.0, z_rstd[:, gs], ALU.mult,
                                         ALU.mult).then_inc(out_bias_done, 1)

            def pair_out(pair):
                g = 2 * pair
                dve.wait_ge(end_rstd_done, pair + 1)
                negative_out_means(slice(g, g + 2))
                dve.tensor_scalar(o_end[:, g, :], xhat[:, g, :], z_mean_var[:, g, 0:1], z_rstd[:, g:g + 1],
                                  ALU.subtract, ALU.mult).then_inc(end_out_done[pair], 1)

            pair_stats(0)
            pair_stats(1)
            pair_scale(0)
            dve.wait_ge(z_rstd_done, last)
            negative_out_means(slice(0, NG))
            dve.wait_ge(turned, KT * groups)
            pair_rows(0)
            pair_scale(1)
            pair_rows(1)
            pair_own_residual(0)
            pair_out_stats(0, 2)
            pair_own_residual(1)
            pair_out_stats(1, 4)
            dve.wait_ge(o_done, NG * last)
            pair_out(0)
            pair_out(1)

        @block.gpsimd
        def _(pool):
            def split_x(grp, k):
                wait(pool, x_hi_done, KT * grp + k + 1)
                pool.tensor_tensor(feat_lo[1][:, k, :], x_raw[:, k, :], feat_hi[1][:, k, :].bitcast(F32),
                                   ALU.subtract).then_inc(feat_ready[0], 1)

            def split_h(grp, k, f=0):
                wait(pool, h_hi_done, KT * grp + k + 1)
                pool.tensor_tensor(feat_lo[f][:, k, :], h_full[:, k, :], feat_hi[f][:, k, :].bitcast(F32),
                                   ALU.subtract).then_inc(feat_ready[1], 1)

            def split_values(n, g):
                pool.wait_ge(v_hi_done, NG * n + g + 1)
                pool.tensor_tensor(v_lo[:, g, 0:H], v_full[:, g, :], v_hi[:, g, 0:H].bitcast(F32),
                                   ALU.subtract).then_inc(v_lo_done, 1)

            def split_weights_of_edges(n, pair):
                pool.wait_ge(p_hi_done, PAIRS * n + pair + 1)
                gs = slice(2 * pair, 2 * pair + 2)
                pool.tensor_tensor(p_lo[:, gs, :], attn[:, gs, :], p_hi[:, gs, :].bitcast(F32),
                                   ALU.subtract).then_inc(p_lo_done, 1)

            def make_masks(t, b, loads):
                if not isinstance(t, int) or t >= 2:
                    pool.wait_ge(masked_done, PAIRS * (2 * t - 1))
                wait(pool, edges_loaded[b], DMA * loads)
                pool.tensor_tensor(masks[b][:].rearrange("p g s i -> p g (s i)"),
                                   edges[b][:].rearrange("p g s i -> p g (s i)"),
                                   triangles[:].rearrange("p s i -> p (s i)").unsqueeze(1).to_broadcast(
                                       [P, NG, SIDES * P]), ALU.mult).then_inc(masks_ready, 1)

            def root(c):
                pool.wait_ge(c_aggr_done, (NG + 1) * (c + 1))
                pool.tensor_tensor(sd[:], mean_var[:, :, 1], half[:], ALU.pow).then_inc(sd_done, 1)

            def scale_and_shift(grp, c, g):
                pool.wait_ge(norm_done, NG * c + g + 1)
                pool.tensor_tensor(z[:, g, :], z[:, g, :], ln_row[:, 0, :], ALU.mult).then_inc(z_scaled, 1)
                pool.wait_ge(z_scaled, NG * grp + g + 1)
                pool.tensor_tensor(z[:, g, :], z[:, g, :], ln_row[:, 1, :], ALU.add).then_inc(z_affine_done, 1)

            def root_out(grp):
                pool.wait_ge(z_aggr_done, (NG + 1) * (grp + 1))
                pool.tensor_tensor(z_rstd[:], z_var[:], minus_half[:], ALU.pow).then_inc(z_rstd_done, 1)

            def phase(n, prev, jobs=(), early=False, late=(), out_grp=None):
                if prev:
                    split_weights_of_edges(n - 1, 1)
                for job in jobs:
                    job()
                for g in range(NG):
                    if g == 2:
                        for job in late:
                            job()
                    split_values(n, g)
                if prev and not early:
                    root(n - 1)
                if out_grp is not None:
                    root_out(out_grp)
                split_weights_of_edges(n, 0)

            def h_lo(grp, f=0):
                return [lambda k=k: split_h(grp, k, f) for k in range(KT)]

            def x_lo(grp):
                return [lambda k=k: split_x(grp, k) for k in range(KT)]

            def first(t):
                if t == 0:
                    pool.memset(ones[:], 1.0).then_inc(blank_done, 1)
                    pool.memset(half[:], 0.5).then_inc(consts_set, 1)
                    pool.memset(minus_half[:], -0.5).then_inc(consts_set, 1)
                    pool.memset(v_lo[:, :, H:VW].bitcast(F32), 0.0).then_inc(consts_set, 1)
                    pool.memset(v_hi[:, :, H + 1:VW].bitcast(F32), 0.0).then_inc(consts_set, 1)
                    pool.memset(v_hi[:, :, H:H + 1].bitcast(F32), 1.0).then_inc(consts_set, 1)
                    pool.wait_ge(blank_done, 1)
                    pool.affine_select(out=triangles[:, 0, :], in_=ones[:], compare_op=ALU.is_ge, fill=0.0, base=0,
                                       pattern=[[-1, P]], channel_multiplier=1).then_inc(consts_set, 1)
                    pool.affine_select(out=triangles[:, 1, :], in_=ones[:], compare_op=ALU.is_gt, fill=0.0, base=0,
                                       pattern=[[1, P]], channel_multiplier=-1).then_inc(consts_set, 1)
                    pool.affine_select(out=identity[:], in_=ones[:], compare_op=ALU.is_equal, fill=0.0, base=0,
                                       pattern=[[-1, P]], channel_multiplier=1).then_inc(consts_set, 1)
                    pool.wait_ge(consts_set, CONSTS)
                    make_masks(0, 0, 1)
                    phase(0, False, late=x_lo(1))
                else:
                    phase(1, True, [lambda: make_masks(1, 1, 1), lambda: root(0)], early=True, late=h_lo(0))
                    phase(2, True, x_lo(2))

            def steady(t, b, half_t):
                n = 2 * t - 1
                phase(n, True, [lambda: make_masks(t, b, half_t + 1)] + h_lo(t - 1))
                affine = [lambda g=g: scale_and_shift(t - 2, n - 1, g) for g in range(NG)]
                if isinstance(t, int) and t == last:
                    phase(n + 1, True, affine[:3] + [lambda: root(n)] + affine[3:], early=True,
                          late=h_lo(last, 1), out_grp=t - 2)
                else:
                    phase(n + 1, True, affine + x_lo(t + 1), out_grp=t - 2)

            each_turn(pool, first, steady)
            end = 2 * last + 1

            def scale_and_shift_end(rows, g, count):
                pool.tensor_tensor(rows[:, g, :], rows[:, g, :], ln_row[:, 0, :], ALU.mult).then_inc(z_scaled, 1)
                pool.wait_ge(z_scaled, count + 1)
                pool.tensor_tensor(rows[:, g, :], rows[:, g, :], ln_row[:, 1, :],
                                   ALU.add).then_inc(z_affine_done, 1)

            before = NG * (last - 1)

            def next_to_last(i):
                pool.wait_ge(norm_done, NG * (end - 1) + i + 1)
                scale_and_shift_end(z, 2 + i, before + i)

            def end_root(pair):
                gs = slice(2 * pair, 2 * pair + 2)
                pool.wait_ge(end_aggr_done, 3 * (pair + 1))
                pool.tensor_tensor(sd[:, gs], mean_var[:, gs, 1], half[:, gs], ALU.pow).then_inc(end_sd_done, 1)

            def end_rows(pair):
                pool.wait_ge(end_norm_done, pair + 1)
                scale_and_shift_end(xhat, 2 * pair + 1, before + 2 + pair)

            phase(end, True, [lambda: root(end - 1), lambda: next_to_last(0), lambda: next_to_last(1)], early=True)
            split_weights_of_edges(end, 1)
            root_out(last - 1)
            end_root(0)
            end_root(1)
            end_rows(0)
            end_rows(1)
            for pair in range(PAIRS):
                gs = slice(2 * pair, 2 * pair + 2)
                pool.wait_ge(end_var_done, 3 * (pair + 1))
                if pair == 0:
                    pool.wait_ge(o_done, NG * last)
                pool.tensor_tensor(z_rstd[:, gs], z_var[:, gs], minus_half[:, gs],
                                   ALU.pow).then_inc(end_rstd_done, 1)


def kernel(x, adj, L0_gnn_W_left, L0_gnn_W_right, L0_gnn_W_lin, L0_gnn_b_lin, L0_gnn_ln_a, L0_gnn_ln_b):
    import concourse.bacc as bacc
    from concourse.bass_utils import run_bass_kernel_spmd

    x, adj = np.asarray(x), np.asarray(adj)
    graphs = x.shape[0]
    groups = graphs // NG
    grouped = x.reshape(groups, NG, P, KT, P)
    a = adj.reshape(groups, NG, P, P)

    def tiles(w):
        return w.reshape(KT, P, H).transpose(1, 0, 2).reshape(P, KT * H)

    left, right, lin = (np.asarray(w) for w in (L0_gnn_W_left, L0_gnn_W_right, L0_gnn_W_lin))
    ln_a, ln_b = np.asarray(L0_gnn_ln_a), np.asarray(L0_gnn_ln_b)
    arrays = {
        "x_t": grouped.transpose(0, 4, 3, 1, 2).reshape(groups, P, KT, NODES),
        "x_rows": x,
        "edges": np.stack([a.transpose(0, 3, 1, 2), a.transpose(0, 2, 1, 3)], axis=3),
        "weights": np.stack([w for l in range(LAYERS) for w in (tiles(left[l]), tiles(right[l]), tiles(lin[l].T))]),
        "ln_cols": np.stack([ln_a[0].reshape(KT, P).T, ln_b[0].reshape(KT, P).T], axis=1),
        "ln_rows": np.stack([ln_a[1], ln_b[1]]),
        "bias_rows": np.asarray(L0_gnn_b_lin),
    }
    arrays = {name: np.ascontiguousarray(v) for name, v in arrays.items()}

    nc = bacc.Bacc("TRN2", target_bir_lowering=False, num_devices=1)
    dram = {name: nc.dram_tensor(name, v.shape, F32, kind="ExternalInput").ap() for name, v in arrays.items()}
    out = nc.dram_tensor("out", (graphs, P, H), F32, kind="ExternalOutput").ap()

    def across(ap, rows):
        return ap.rearrange("a n -> (a n)").partition_broadcast(P).rearrange("p (a n) -> p a n", a=rows)

    build_gnn(nc, dram["x_t"], dram["x_rows"].rearrange("(t g) i o -> t i g o", g=NG), dram["edges"],
              dram["weights"], dram["ln_cols"], across(dram["ln_rows"], 2), across(dram["bias_rows"], LAYERS),
              out.rearrange("(t g) i o -> t i g o", g=NG))
    result = run_bass_kernel_spmd(nc, [arrays], core_ids=[0])
    return result.results[0]["out"]
```
